# Optimizing a Trainium2 kernel written in Bass

```python
import numpy as np
import jax
import jax.numpy as jnp

def _softmax(x, axis=-1):
    return jax.nn.softmax(x, axis=axis)

def _gelu(x):
    return jax.nn.gelu(x, approximate=True)

def _silu(x):
    return jax.nn.silu(x)

def _sigmoid(x):
    return jax.nn.sigmoid(x)

def _layernorm(x, axis=-1, eps=1e-05):
    m = jnp.mean(x, axis=axis, keepdims=True)
    v = jnp.var(x, axis=axis, keepdims=True)
    return (x - m) / jnp.sqrt(v + eps)

def _scatter_add(tgt, idx, src, axis=0):
    return tgt.at[idx].add(src)

def _segment_sum(src, seg, n):
    return jax.ops.segment_sum(src, seg, n)
kernel_name = 'mk_rec_standalone_d1_rec_r8_9b2f77'

def setup_inputs(seed: int=0):
    np.random.seed(seed)
    _w = jnp.asarray

    def _rec_inputs():
        import jax
        import jax.numpy as jnp
        _rk = jax.random.key(seed)
        r_target_key = -0.00154741 + 1.00114 * jax.random.normal(jax.random.fold_in(_rk, 1), (2048, 64), jnp.float32)
        r_item_keys = -0.00010897 + 0.999902 * jax.random.normal(jax.random.fold_in(_rk, 2), (2048, 200, 64), jnp.float32)
        r_item_values = 0.000157846 + 1.00013 * jax.random.normal(jax.random.fold_in(_rk, 3), (2048, 200, 64), jnp.float32)
        r_mask = jax.random.randint(jax.random.fold_in(_rk, 4), (2048, 200), 0, 2, jnp.int32)
        return (r_target_key, r_item_keys, r_item_values, r_mask)
    r_target_key, r_item_keys, r_item_values, r_mask = _rec_inputs()

    def _L0_rec_setup():
        import jax, jax.numpy as jnp
        import numpy as np
        B, L, D = (512, 200, 64)
        key = jax.random.key(seed)
        ks = jax.random.split(key, 7)
        target_key = jax.random.normal(ks[0], (B, D), dtype=jnp.float32)
        item_keys = jax.random.normal(ks[1], (B, L, D), dtype=jnp.float32)
        item_values = jax.random.normal(ks[2], (B, L, D), dtype=jnp.float32)
        mask = jax.random.randint(ks[3], (B, L), 0, 2, dtype=jnp.int32)
        scale = 1.0 / np.sqrt(D)
        W_target = jax.random.uniform(ks[4], (D, D), jnp.float32, -scale, scale)
        W_item = jax.random.uniform(ks[5], (D, D), jnp.float32, -scale, scale)
        W_value = jax.random.uniform(ks[6], (D, D), jnp.float32, -scale, scale)
        return {'target_key': target_key, 'item_keys': item_keys, 'item_values': item_values, 'mask': mask, 'W_target': W_target, 'W_item': W_item, 'W_value': W_value}
    _L0_rec_all = _L0_rec_setup()
    _L0_rec_in = {k: v for k, v in _L0_rec_all.items() if k in ('W_target', 'W_item', 'W_value')}
    del _L0_rec_all
    return {'r_target_key': r_target_key, 'r_item_keys': r_item_keys, 'r_item_values': r_item_values, 'r_mask': r_mask, 'L0_rec_W_target': _L0_rec_in['W_target'], 'L0_rec_W_item': _L0_rec_in['W_item'], 'L0_rec_W_value': _L0_rec_in['W_value']}

def reference(r_target_key, r_item_keys, r_item_values, r_mask, L0_rec_W_target, L0_rec_W_item, L0_rec_W_value):
    import jax
    import jax.numpy as jnp

    def _L0_rec_ref(target_key, item_keys, item_values, mask, W_target, W_item, W_value):
        import jax, jax.numpy as jnp
        import numpy as np
        B, L, D = (512, 200, 64)
        scaler = jnp.float32(D) ** 0.5
        q = target_key @ W_target.T
        k = jnp.einsum('bld,ed->ble', item_keys, W_item)
        v = jnp.einsum('bld,ed->ble', item_values, W_value)
        scores = jnp.einsum('bd,bld->bl', q, k) / scaler
        scores = scores + -100000000.0 * (1.0 - mask.astype(scores.dtype))
        w = jax.nn.softmax(scores, axis=1)
        return jnp.einsum('bl,bld->bd', w, v)
    y = _L0_rec_ref(r_target_key, r_item_keys, r_item_values, r_mask, L0_rec_W_target, L0_rec_W_item, L0_rec_W_value)
    return y

_drawn_inputs = setup_inputs


def setup_inputs(seed=0):
    import zlib

    import numpy as np

    out = dict(_drawn_inputs(seed))
    spreads = {}
    factors = {}
    for name, (base, spread) in spreads.items():
        noise = np.random.default_rng([zlib.crc32(name.encode()), seed]).standard_normal(out[name].shape)
        drawn = base * np.exp(spread * noise) if base else spread * noise
        out[name] = jnp.asarray(drawn.astype(out[name].dtype))
    for name, factor in factors.items():
        out[name] = (out[name] * factor).astype(out[name].dtype)
    return out
```

```python
import concourse.bass as bass
from concourse import mybir
from contextlib import ExitStack


def target_attention(nc, target, keys, values, mask, w_target, w_item, w_value, out):
    fp32 = mybir.dt.float32
    int32 = mybir.dt.int32
    ALU = mybir.AluOpType
    ACT = mybir.ActivationFunctionType
    AX = mybir.AxisListType

    B, L, D = keys.shape
    P = 128
    PARTS = 8
    TB = P // PARTS
    LI = L // PARTS
    ROW = LI * D
    HT, ST, RT = 2, 4, 8
    HALVES = RT // HT
    ROUNDS = B // (TB * RT)
    J = 5
    GROUPS = LI // J
    JM, JD = J * TB, J * D
    SQ = 32
    SCALE = float(D) ** -0.5
    MASKED = 100000000.0

    assert LI % J == 0 and JM <= P and JD <= 512 and ROUNDS * RT * TB == B

    keys_v = keys.rearrange("b (o i) d -> (b o) (i d)", o=PARTS).rearrange(
        "(c t p) x -> c p t x", p=P, t=HT)
    values_v = values.rearrange("b (o i) d -> (b o) (i d)", o=PARTS).rearrange(
        "(c t p) x -> c p t x", p=P, t=HT)
    mask_v = mask.rearrange("b (o i) -> (b o) i", o=PARTS).rearrange("(r t p) i -> r p t i", p=P, t=RT)
    target_v = target.rearrange("(r b) d -> b r d", b=P)
    out_v = out.rearrange("(r b) d -> r b d", b=P)

    ctx = ExitStack()
    with ctx:
        def sb(name, shape, dt=fp32):
            return ctx.enter_context(nc.sbuf_tensor(name, shape, dt))

        def ps(name):
            return ctx.enter_context(nc.psum_tensor(name, [P, 512], fp32))

        def sem(name):
            return ctx.enter_context(nc.semaphore(name))

        key_sb = [sb(f"key{j}", [P, HT, LI, D]) for j in range(HALVES)]
        value_sb = [sb(f"value{j}", [P, HT, LI * D]) for j in range(HALVES)]
        mask_raw = sb("mask_raw", [P, RT, LI], int32)
        mask_bias = sb("mask_bias", [P, 2, ST * LI])
        dots = sb("dots", [P, 2, ST * LI])
        scores = sb("scores", [P, 2, ST, LI])
        peak = sb("peak", [P, 2, SQ])
        peak_t = sb("peak_t", [P, 2, SQ])
        batch_peak = sb("batch_peak", [P, 2, SQ // PARTS])
        shift = sb("shift", [P, 2, SQ])
        weights = sb("weights", [P, 2, ST, LI])
        weight_sum = sb("weight_sum", [P, 2, ST])
        spread = sb("spread", [P, 2, ST, LI, TB])
        recip = sb("recip", [JM, 2, ST])
        crossed = sb("crossed", [JM, 2, JD])
        mixed = sb("mixed", [D, P])
        out_sb = sb("out_sb", [P, D])
        target_sb = sb("target_sb", [P, ROUNDS, D])
        target_t = sb("target_t", [D, ROUNDS * P])
        target_rep = sb("target_rep", [D, P, PARTS])
        wt_sb = sb("wt_sb", [D, D])
        wi_sb = sb("wi_sb", [D, D])
        wv_sb = sb("wv_sb", [D, D])
        w_query = sb("w_query", [D, D])
        wv_t = sb("wv_t", [D, D])
        ident = sb("ident", [P, P])
        own = sb("own", [P, TB])
        own_rep = sb("own_rep", [P, J, TB])

        query = [ps("query0"), ps("query1")]
        cross = [ps("cross0"), ps("cross1")]
        mixed_ps, denom_ps, out_ps = ps("mixed_ps"), ps("denom_ps"), ps("out_ps")

        keys_in = [sem(f"keys_in{j}") for j in range(HALVES)]
        values_in = [sem(f"values_in{j}") for j in range(HALVES)]
        mask_in, weights_in, target_in, target_rest_in = (
            sem("mask_in"), sem("weights_in"), sem("target_in"), sem("target_rest_in"))
        ident_zero, ident_ready = sem("ident_zero"), sem("ident_ready")
        own_ready, own_rep_ready, peak_clear = sem("own_ready"), sem("own_rep_ready"), sem("peak_clear")
        folded, turned_wv, turned_target = sem("folded"), sem("turned_wv"), sem("turned_target")
        folded_copied, wv_copied, target_copied = (
            sem("folded_copied"), sem("wv_copied"), sem("target_copied"))
        target_spread = sem("target_spread")
        query_ready = sem("query_ready")
        multiplied, summed = sem("multiplied"), sem("summed")
        bias_ready, masked, peaked, turned, grouped, shift_ready = (
            sem("bias_ready"), sem("masked"), sem("peaked"), sem("turned"), sem("grouped"),
            sem("shift_ready"))
        exps_ready = sem("exps_ready")
        spread_ready = sem("spread_ready")
        denom_ready, recip_ready = sem("denom_ready"), sem("recip_ready")
        cross_ready, cross_copied, picked = sem("cross_ready"), sem("cross_copied"), sem("picked")
        mixed_copied, out_ready, out_copied, out_stored = (
            sem("mixed_copied"), sem("out_ready"), sem("out_copied"), sem("out_stored"))

        block = ctx.enter_context(nc.Block())

        def rounds(engine, body):
            body(0, first=True, last=False)
            with engine.Fori(1, ROUNDS - 1) as r:
                body(r, first=False, last=False)
            body(ROUNDS - 1, first=False, last=True)

        @block.sync
        def _(sp):
            def load_keys(r, j, first):
                if not first:
                    sp.wait_ge(summed, HALVES * (r - 1) + j + 1)
                sp.dma_start(key_sb[j][:, :, :, :].rearrange("p t i d -> p t (i d)"),
                             keys_v[HALVES * r + j]).then_inc(keys_in[j], 16)

            def load_mask(r, first):
                if not first:
                    sp.wait_ge(bias_ready, 2 * r)
                sp.dma_start(mask_raw[:, :, :], mask_v[r]).then_inc(mask_in, 16)

            def body(r, first, last):
                for j in range(HALVES):
                    if j < HALVES - 2:
                        load_keys(r, j + 2, first)
                    elif not last:
                        load_keys(r + 1, j + 2 - HALVES, False)
                    if not first:
                        sp.wait_ge(cross_ready, RT * (r - 1) + HT * (j + 1))
                    sp.dma_start(value_sb[j][:, :, :], values_v[HALVES * r + j]).then_inc(values_in[j], 16)
                    if j == 1 and not last:
                        load_mask(r + 1, False)

            load_keys(0, 0, True)
            load_mask(0, True)
            load_keys(0, 1, True)
            sp.dma_start(target_sb[:, ROUNDS // 4:, :], target_v[:, ROUNDS // 4:, :]).then_inc(target_rest_in, 16)
            rounds(sp, body)

        @block.gpsimd
        def _(pool):
            nc.gpsimd.memset(ident[:, :], 0.0).then_inc(ident_zero, 1)
            pool.wait_ge(ident_zero, 1)
            nc.gpsimd.affine_select(out=ident[:, :], in_=ident[:, :], compare_op=ALU.not_equal, fill=1.0,
                                    base=0, pattern=[[-1, P]], channel_multiplier=1).then_inc(ident_ready, 1)

            def body(r, first, last):
                for k in range(2):
                    for h in range(2):
                        pool.wait_ge(exps_ready, RT * r + ST * k + HT * (h + 1))
                        if not first:
                            pool.wait_ge(cross_ready, RT * (r - 1) + ST * k + HT * (h + 1))
                        t0 = HT * h
                        w = weights[:, k, t0:t0 + HT, :].rearrange("p t i -> p (t i)")
                        nc.gpsimd.tensor_tensor(
                            spread[:, k, t0:t0 + HT, :, :].rearrange("p t i m -> p (t i) m"),
                            w.unsqueeze(2).to_broadcast([P, HT * LI, TB]),
                            own[:, :].unsqueeze(1).to_broadcast([P, HT * LI, TB]),
                            ALU.mult).then_inc(spread_ready, 1)

            pool.wait_ge(own_ready, 1)
            rounds(pool, body)

        @block.vector
        def _(dve):
            nc.vector.memset(peak[:, :, :], 0.0).then_inc(peak_clear, 1)
            dve.wait_ge(ident_ready, 1)
            nc.vector.tensor_reduce(out=own[:, :], in_=ident[:, :].rearrange("p (m o) -> p m o", o=PARTS),
                                    axis=AX.X, op=ALU.add).then_inc(own_ready, 1)
            dve.wait_ge(own_ready, 1)
            nc.vector.tensor_copy(own_rep[:, :, :],
                                  own[:, :].unsqueeze(1).to_broadcast([P, J, TB])).then_inc(own_rep_ready, 1)
            dve.wait_ge(peak_clear, 1)

            def invert(r, k, first):
                dve.wait_ge(denom_ready, 2 * r + k + 1)
                if not first:
                    dve.wait_ge(cross_copied, RT * (r - 1) + ST * (k + 1))
                nc.vector.reciprocal(recip[:, k, :], denom_ps[0:JM, ST * k:ST * (k + 1)]).then_inc(recip_ready, 1)

            def body(r, first, last):
                for k in range(2):
                    step = 2 * r + k
                    for h in range(2):
                        j = 2 * k + h
                        half = HALVES * r + j
                        dve.wait_ge(keys_in[j], 16 * (r + 1))
                        if h == 0:
                            dve.wait_ge(query_ready, step + 1)
                        q = query[k][:, h * HT * D:(h + 1) * HT * D].rearrange("p (t d) -> p t d", t=HT)
                        nc.vector.tensor_tensor(key_sb[j][:, :, :, :], key_sb[j][:, :, :, :],
                                                q.unsqueeze(2).to_broadcast([P, HT, LI, D]),
                                                ALU.mult).then_inc(multiplied, 1)
                        dve.wait_ge(multiplied, half + 1)
                        nc.vector.tensor_reduce(out=dots[:, k, h * HT * LI:(h + 1) * HT * LI],
                                                in_=key_sb[j][:, :, :, :].rearrange("p t i d -> p (t i) d"),
                                                axis=AX.X, op=ALU.add).then_inc(summed, 1)
                        if h == 0 and k == 1:
                            invert(r, 0, first)
                        elif h == 0 and not first:
                            invert(r - 1, 1, False) if not isinstance(r, int) or r > 1 else invert(r - 1, 1, True)
                    dve.wait_ge(summed, HALVES * r + 2 * k + 2)
                    dve.wait_ge(bias_ready, step + 1)
                    if not first:
                        dve.wait_ge(exps_ready, RT * (r - 1) + ST * (k + 1))
                    nc.vector.scalar_tensor_tensor(
                        out=scores[:, k, :, :].rearrange("p t i -> p (t i)"), in0=dots[:, k, :], scalar=SCALE,
                        in1=mask_bias[:, k, :], op0=ALU.mult, op1=ALU.add).then_inc(masked, 1)
                    dve.wait_ge(masked, step + 1)
                    nc.vector.tensor_reduce(out=peak[:, k, 0:ST], in_=scores[:, k, :, :],
                                            axis=AX.X, op=ALU.max).then_inc(peaked, 1)
                    dve.wait_ge(peaked, step + 1)
                    nc.vector.transpose(peak_t[:, k, :], peak[:, k, :]).then_inc(turned, 1)
                    dve.wait_ge(turned, step + 1)
                    nc.vector.tensor_reduce(out=batch_peak[:, k, :],
                                            in_=peak_t[:, k, :].rearrange("p (m o) -> p m o", o=PARTS),
                                            axis=AX.X, op=ALU.max, negate=True).then_inc(grouped, 1)
                    dve.wait_ge(grouped, step + 1)
                    nc.vector.transpose(shift[:, k, :],
                                        batch_peak[:, k, :].unsqueeze(2).to_broadcast([P, SQ // PARTS, PARTS])
                                        ).then_inc(shift_ready, 1)

            rounds(dve, body)
            invert(ROUNDS - 1, 1, False)

        @block.scalar
        def _(act):
            act.dma_start(wt_sb[:, :], w_target).then_inc(weights_in, 16)
            act.dma_start(wi_sb[:, :], w_item).then_inc(weights_in, 16)
            act.dma_start(wv_sb[:, :], w_value).then_inc(weights_in, 16)
            act.dma_start(target_sb[:, 0:ROUNDS // 4, :], target_v[:, 0:ROUNDS // 4, :]).then_inc(target_in, 16)

            act.wait_ge(folded, 1)
            nc.scalar.copy(w_query[:, :], denom_ps[0:D, 0:D]).then_inc(folded_copied, 1)

            def copy_target(n):
                act.wait_ge(turned_target, n + 1)
                nc.scalar.copy(target_t[:, n * 512:(n + 1) * 512], cross[n % 2][0:D, :]).then_inc(target_copied, 1)

            def spread_target(r, cols, first):
                if not first:
                    act.wait_ge(query_ready, 2 * r)
                nc.scalar.copy(target_rep[:, :, :],
                               cols.unsqueeze(2).to_broadcast([D, P, PARTS])).then_inc(target_spread, 1)

            def convert_mask(r, k, first):
                if k == 0:
                    act.wait_ge(mask_in, 16 * (r + 1))
                if not first:
                    act.wait_ge(masked, 2 * r + k - 1)
                nc.scalar.activation(mask_bias[:, k, :],
                                     mask_raw[:, ST * k:ST * (k + 1), :].rearrange("p t i -> p (t i)"),
                                     ACT.Copy, bias=-MASKED, scale=MASKED).then_inc(bias_ready, 1)

            convert_mask(0, 0, True)
            convert_mask(0, 1, True)
            copy_target(0)
            act.wait_ge(target_copied, 1)
            spread_target(0, target_t[:, 0:P], True)
            for n in range(1, ROUNDS // 4):
                copy_target(n)
            act.wait_ge(turned_wv, 1)
            nc.scalar.copy(wv_t[:, :], out_ps[0:D, 0:D]).then_inc(wv_copied, 1)
            act.wait_ge(target_copied, ROUNDS // 4)

            def body(r, first, last):
                if not last:
                    spread_target(r + 1, target_t[:, bass.ds((r + 1) * P, P)], False)
                for k in range(2):
                    step = 2 * r + k
                    act.wait_ge(shift_ready, step + 1)
                    if not first:
                        act.wait_ge(spread_ready, HALVES * (r - 1) + 2 * (k + 1))
                        act.wait_ge(denom_ready, 2 * (r - 1) + k + 1)
                    for t in range(ST):
                        nc.scalar.activation(weights[:, k, t, :], scores[:, k, t, :], ACT.Exp,
                                             bias=shift[:, k, t:t + 1], scale=1.0,
                                             accum_out=weight_sum[:, k, t:t + 1]).then_inc(exps_ready, 1)
                    if not last:
                        convert_mask(r + 1, k, False)
                    for t in range(ST):
                        tile = RT * r + ST * k + t
                        act.wait_ge(cross_ready, tile + 1)
                        if t == 0:
                            act.wait_ge(recip_ready, step + 1)
                        if not (first and k == 0 and t < 2):
                            act.wait_ge(picked, tile - 1)
                        nc.scalar.mul(crossed[:, t % 2, :], cross[t % 2][0:JM, 0:JD],
                                      recip[:, k, t:t + 1]).then_inc(cross_copied, 1)
                act.wait_ge(picked, RT * (r + 1))
                if not first:
                    act.wait_ge(out_ready, r)
                nc.scalar.copy(mixed[:, :], mixed_ps[0:D, 0:P]).then_inc(mixed_copied, 1)
                act.wait_ge(out_ready, r + 1)
                if not first:
                    act.wait_ge(out_stored, 16 * r)
                nc.scalar.copy(out_sb[:, :], out_ps[:, 0:D]).then_inc(out_copied, 1)
                act.wait_ge(out_copied, r + 1)
                act.dma_start(out_v[r], out_sb[:, :]).then_inc(out_stored, 16)

            rounds(act, body)
            act.wait_ge(out_stored, 16 * ROUNDS)

        @block.tensor
        def _(pe):
            def make_query(r, k, first):
                if k == 0:
                    pe.wait_ge(target_spread, r + 1)
                if not first:
                    pe.wait_ge(multiplied, HALVES * (r - 1) + 2 * (k + 1))
                for t in range(ST):
                    b0 = (ST * k + t) * TB
                    last = nc.tensor.matmul(query[k][:, t * D:(t + 1) * D],
                                            target_rep[:, b0:b0 + TB, :].rearrange("d b o -> d (b o)"),
                                            w_query[:, :], start=True, stop=True)
                last.then_inc(query_ready, 1)

            def turn_target(n):
                if n >= 2:
                    pe.wait_ge(target_copied, n - 1)
                for x in range(4):
                    last = nc.tensor.transpose(cross[n % 2][0:D, x * P:(x + 1) * P],
                                               target_sb[:, 4 * n + x, :], ident[:, :])
                last.then_inc(turned_target, 1)

            pe.wait_ge(ident_ready, 1)
            pe.wait_ge(weights_in, 48)
            nc.tensor.matmul(denom_ps[0:D, 0:D], wt_sb[:, :], wi_sb[:, :], start=True, stop=True).then_inc(folded, 1)
            nc.tensor.transpose(out_ps[0:D, 0:D], wv_sb[:, :], ident[0:D, 0:D]).then_inc(turned_wv, 1)
            pe.wait_ge(target_in, 16)
            turn_target(0)
            pe.wait_ge(folded_copied, 1)
            make_query(0, 0, True)
            make_query(0, 1, True)
            pe.wait_ge(target_rest_in, 16)
            for n in range(1, ROUNDS // 4):
                turn_target(n)
            pe.wait_ge(target_copied, ROUNDS // 4)
            pe.wait_ge(wv_copied, 1)
            pe.wait_ge(own_rep_ready, 1)

            def cross_products(r, k, t, first):
                tile = RT * r + ST * k + t
                j, h = 2 * k + t // HT, t // HT
                if t % HT == 0:
                    pe.wait_ge(spread_ready, HALVES * r + j + 1)
                    pe.wait_ge(values_in[j], 16 * (r + 1))
                if not (first and k == 0 and t < 2):
                    pe.wait_ge(cross_copied, tile - 1)
                for g in range(GROUPS):
                    last = nc.tensor.matmul(
                        cross[t % 2][0:JM, 0:JD],
                        spread[:, k, t, g * J:(g + 1) * J, :].rearrange("p i m -> p (i m)"),
                        value_sb[j][:, t % HT, g * JD:(g + 1) * JD], start=(g == 0), stop=(g == GROUPS - 1))
                last.then_inc(cross_ready, 1)

            def pick(r, k, t, first):
                tile = RT * r + ST * k + t
                pe.wait_ge(cross_copied, tile + 1)
                if k == 0 and t == 0 and not first:
                    pe.wait_ge(mixed_copied, r)
                b0 = (ST * k + t) * TB
                for x in range(J):
                    last = nc.tensor.matmul(mixed_ps[0:D, b0:b0 + TB], crossed[:, t % 2, x * D:(x + 1) * D],
                                            ident[0:JM, x * TB:(x + 1) * TB], start=(x == 0), stop=(x == J - 1))
                last.then_inc(picked, 1)

            def body(r, first, last):
                for k in range(2):
                    if not last:
                        make_query(r + 1, k, False)
                    pe.wait_ge(exps_ready, RT * r + ST * (k + 1))
                    if not (first and k == 0):
                        pe.wait_ge(recip_ready, 2 * r + k)
                    nc.tensor.matmul(denom_ps[0:JM, ST * k:ST * (k + 1)],
                                     own_rep[:, :, :].rearrange("p j m -> p (j m)"),
                                     weight_sum[:, k, :], start=True, stop=True).then_inc(denom_ready, 1)
                    for t in range(ST):
                        cross_products(r, k, t, first)
                        if t > 0:
                            pick(r, k, t - 1, first)
                    pick(r, k, ST - 1, first)
                pe.wait_ge(mixed_copied, r + 1)
                if not first:
                    pe.wait_ge(out_copied, r)
                nc.tensor.matmul(out_ps[:, 0:D], mixed[:, :], wv_t[:, :], start=True, stop=True).then_inc(out_ready, 1)

            rounds(pe, body)


_INS = ["r_target_key", "r_item_keys", "r_item_values", "r_mask",
        "L0_rec_W_target", "L0_rec_W_item", "L0_rec_W_value"]


def kernel(**inputs):
    import numpy as np
    import concourse.bacc as bacc
    from concourse.bass_utils import run_bass_kernel_spmd

    nc = bacc.Bacc("TRN2", target_bir_lowering=False, num_devices=1)
    arrays, args = {}, []
    for name in _INS:
        a = np.ascontiguousarray(inputs[name])
        arrays[f"in_{name}"] = a
        args.append(nc.dram_tensor(f"in_{name}", a.shape, mybir.dt.from_np(a.dtype), kind="ExternalInput").ap())
    out = nc.dram_tensor("out", inputs["r_target_key"].shape, mybir.dt.float32, kind="ExternalOutput").ap()
    target_attention(nc, *args, out)
    r = run_bass_kernel_spmd(nc, [arrays], core_ids=[0])
    return r.results[0]["out"]
```

```python
import concourse.bass as bass
from concourse import mybir
from contextlib import ExitStack


def target_attention(nc, target, keys, values, mask, w_target, w_item, w_value, out):
    fp32 = mybir.dt.float32
    int32 = mybir.dt.int32
    ALU = mybir.AluOpType
    ACT = mybir.ActivationFunctionType
    AX = mybir.AxisListType

    B, L, D = keys.shape
    P = 128
    PARTS = 8
    TB = P // PARTS
    LI = L // PARTS
    ROW = LI * D
    HT, ST, RT = 2, 4, 8
    HALVES = RT // HT
    ROUNDS = B // (TB * RT)
    LEAD = 3
    LATE = (3, 5, 7)
    J = 5
    GROUPS = LI // J
    JM, JD = J * TB, J * D
    SQ = 32
    SCALE = float(D) ** -0.5
    MASKED = 100000000.0

    assert LI % J == 0 and JM <= P and JD <= 512 and ROUNDS * RT * TB == B

    keys_v = keys.rearrange("b (o i) d -> (b o) (i d)", o=PARTS).rearrange(
        "(c t p) x -> c p t x", p=P, t=HT)
    values_v = values.rearrange("b (o i) d -> (b o) (i d)", o=PARTS).rearrange(
        "(c t p) x -> c p t x", p=P, t=HT)
    RUN_PARTS = 8
    RUN = RUN_PARTS * LI
    MP = P // RUN_PARTS
    mask_v = mask.rearrange("(r t m) (q x) -> r (m q) t x", t=RT, m=TB, x=RUN)
    HEAD = 4
    REST = ROUNDS - HEAD
    target_head = target[0:P * HEAD, :].rearrange("(p x) d -> p x d", x=HEAD)
    target_rest = target[P * HEAD:, :].rearrange("(p x) d -> p x d", x=REST)
    out_v = out.rearrange("(r b) d -> r b d", b=P)

    ctx = ExitStack()
    with ctx:
        def sb(name, shape, dt=fp32):
            return ctx.enter_context(nc.sbuf_tensor(name, shape, dt))

        def ps(name):
            return ctx.enter_context(nc.psum_tensor(name, [P, 512], fp32))

        def sem(name):
            return ctx.enter_context(nc.semaphore(name))

        key_sb = [sb(f"key{j}", [P, HT, LI, D]) for j in range(HALVES)]
        value_sb = [sb(f"value{j}", [P, HT, LI * D]) for j in range(HALVES)]
        mask_raw = sb("mask_raw", [MP, RT, RUN], int32)
        mask_f = sb("mask_f", [MP, RT, RUN])
        place = sb("place", [MP, RUN_PARTS, P])
        mask_bias = sb("mask_bias", [P, 2, ST * LI])
        dots = sb("dots", [P, 2, ST * LI])
        scores = sb("scores", [P, 2, ST, LI])
        peak = sb("peak", [P, 2, SQ])
        peak_t = sb("peak_t", [P, 2, SQ])
        batch_peak = sb("batch_peak", [P, 2, SQ // PARTS])
        shift = sb("shift", [P, 2, SQ])
        weights = sb("weights", [P, 2, ST, LI])
        weight_sum = sb("weight_sum", [P, 2, ST])
        spread = sb("spread", [P, 2, ST, LI, TB])
        recip = sb("recip", [JM, 2, ST])
        crossed = sb("crossed", [JM, 2, JD])
        mixed = sb("mixed", [D, P])
        out_sb = sb("out_sb", [P, D])
        partial = sb("partial", [P, len(LATE), D])
        target_sb = sb("target_sb", [P, ROUNDS, D])
        target_t = sb("target_t", [D, ROUNDS * P])
        target_rep = sb("target_rep", [D, 2, P // 2, PARTS])
        wt_sb = sb("wt_sb", [D, D])
        wi_sb = sb("wi_sb", [D, D])
        wv_sb = sb("wv_sb", [D, D])
        w_query = sb("w_query", [D, D])
        wv_t = sb("wv_t", [D, D])
        ident = sb("ident", [P, P])
        own = sb("own", [P, TB])
        own_rep = sb("own_rep", [P, J, TB])

        query = [ps("query0"), ps("query1")]
        cross = [ps("cross0"), ps("cross1")]
        mixed_ps, denom_ps, out_ps = ps("mixed_ps"), ps("denom_ps"), ps("out_ps")
        mask_ps = ps("mask_ps")

        keys_in = [sem(f"keys_in{j}") for j in range(HALVES)]
        values_in = [sem(f"values_in{j}") for j in range(HALVES)]
        mask_in, weights_in, wv_in, target_in, target_rest_in = (
            sem("mask_in"), sem("weights_in"), sem("wv_in"), sem("target_in"), sem("target_rest_in"))
        ident_zero, ident_ready = sem("ident_zero"), sem("ident_ready")
        place_zero, place_ready = sem("place_zero"), sem("place_ready")
        mask_cast, mask_placed = sem("mask_cast"), sem("mask_placed")
        own_ready, own_rep_ready, peak_clear = sem("own_ready"), sem("own_rep_ready"), sem("peak_clear")
        folded, turned_wv, turned_target = sem("folded"), sem("turned_wv"), sem("turned_target")
        folded_copied, wv_copied, target_copied = (
            sem("folded_copied"), sem("wv_copied"), sem("target_copied"))
        target_spread = sem("target_spread")
        query_ready = sem("query_ready")
        multiplied, summed = sem("multiplied"), sem("summed")
        bias_ready, masked, peaked, turned, grouped, shift_ready = (
            sem("bias_ready"), sem("masked"), sem("peaked"), sem("turned"), sem("grouped"),
            sem("shift_ready"))
        exps_ready = sem("exps_ready")
        late_weights = sem("late_weights")
        weighted, partial_ready = sem("weighted"), sem("partial_ready")
        spread_ready = sem("spread_ready")
        denom_ready, recip_ready = sem("denom_ready"), sem("recip_ready")
        cross_ready, cross_copied, picked = sem("cross_ready"), sem("cross_copied"), sem("picked")
        mixed_copied, out_ready, out_copied, out_stored = (
            sem("mixed_copied"), sem("out_ready"), sem("out_copied"), sem("out_stored"))

        block = ctx.enter_context(nc.Block())

        def rounds(engine, body):
            body(0, first=True, left=2)
            with engine.Fori(1, ROUNDS - 2) as r:
                body(r, first=False, left=2)
            body(ROUNDS - 2, first=False, left=1)
            body(ROUNDS - 1, first=False, left=0)

        def late(left, k, t):
            return left == 0 and ST * k + t in LATE

        @block.sync
        def _(sp):
            def load_keys(r, j, first):
                if not first:
                    sp.wait_ge(summed, HALVES * (r - 1) + j + 1)
                sp.dma_start(key_sb[j][:, :, :, :].rearrange("p t i d -> p t (i d)"),
                             keys_v[HALVES * r + j]).then_inc(keys_in[j], 16)

            def load_mask(r, first):
                if not first:
                    sp.wait_ge(mask_cast, r)
                sp.dma_start(mask_raw[:, :, :], mask_v[r]).then_inc(mask_in, 16)

            def body(r, first, left):
                for j in range(HALVES):
                    if j + LEAD < HALVES:
                        load_keys(r, j + LEAD, first)
                    elif left:
                        load_keys(r + 1, j + LEAD - HALVES, False)
                    if not first:
                        sp.wait_ge(cross_ready, RT * (r - 1) + HT * (j + 1))
                    sp.dma_start(value_sb[j][:, :, :], values_v[HALVES * r + j]).then_inc(values_in[j], 16)
                if left == 2:
                    load_mask(r + 2, False)

            load_keys(0, 0, True)
            sp.dma_start(target_sb[:, 0:HEAD, :], target_head).then_inc(target_in, 16)
            sp.dma_start(wt_sb[:, :], w_target).then_inc(weights_in, 16)
            sp.dma_start(wi_sb[:, :], w_item).then_inc(weights_in, 16)
            load_mask(0, True)
            load_keys(0, 1, True)
            sp.dma_start(target_sb[:, HEAD:, :], target_rest).then_inc(target_rest_in, 16)
            sp.dma_start(wv_sb[:, :], w_value).then_inc(wv_in, 16)
            for j in range(2, LEAD):
                load_keys(0, j, True)
            load_mask(1, False)
            rounds(sp, body)

        @block.gpsimd
        def _(pool):
            nc.gpsimd.memset(ident[:, :], 0.0).then_inc(ident_zero, 1)
            pool.wait_ge(ident_zero, 1)
            nc.gpsimd.affine_select(out=ident[:, :], in_=ident[:, :], compare_op=ALU.not_equal, fill=1.0,
                                    base=0, pattern=[[-1, P]], channel_multiplier=1).then_inc(ident_ready, 1)
            nc.gpsimd.memset(place[:, :, :], 0.0).then_inc(place_zero, 1)
            pool.wait_ge(place_zero, 1)
            nc.gpsimd.affine_select(out=place[:, :, :], in_=place[:, :, :], compare_op=ALU.not_equal, fill=1.0,
                                    base=0, pattern=[[1, RUN_PARTS], [-1, P]], channel_multiplier=RUN_PARTS).then_inc(place_ready, 1)

            def body(r, first, left):
                for k in range(2):
                    for h in range(2):
                        pool.wait_ge(exps_ready, RT * r + ST * k + HT * (h + 1))
                        if not first:
                            pool.wait_ge(cross_ready, RT * (r - 1) + ST * k + HT * (h + 1))
                        t0 = HT * h
                        n = 1 if not left and ST * k + t0 + 1 in LATE else HT
                        w = weights[:, k, t0:t0 + n, :].rearrange("p t i -> p (t i)")
                        nc.gpsimd.tensor_tensor(
                            spread[:, k, t0:t0 + n, :, :].rearrange("p t i m -> p (t i) m"),
                            w.unsqueeze(2).to_broadcast([P, n * LI, TB]),
                            own[:, :].unsqueeze(1).to_broadcast([P, n * LI, TB]),
                            ALU.mult).then_inc(spread_ready, 1)

            pool.wait_ge(own_ready, 1)
            rounds(pool, body)

        @block.vector
        def _(dve):
            nc.vector.memset(peak[:, :, :], 0.0).then_inc(peak_clear, 1)
            dve.wait_ge(ident_ready, 1)
            nc.vector.tensor_reduce(out=own[:, :], in_=ident[:, :].rearrange("p (m o) -> p m o", o=PARTS),
                                    axis=AX.X, op=ALU.add).then_inc(own_ready, 1)
            dve.wait_ge(own_ready, 1)
            nc.vector.tensor_copy(own_rep[:, :, :],
                                  own[:, :].unsqueeze(1).to_broadcast([P, J, TB])).then_inc(own_rep_ready, 1)
            dve.wait_ge(peak_clear, 1)

            def invert(r, k):
                dve.wait_ge(denom_ready, 2 * r + k + 1)
                nc.vector.reciprocal(recip[:, k, :], denom_ps[0:JM, ST * k:ST * (k + 1)]).then_inc(recip_ready, 1)

            def body(r, first, left):
                for k in range(2):
                    step = 2 * r + k
                    for h in range(2):
                        j = 2 * k + h
                        half = HALVES * r + j
                        dve.wait_ge(keys_in[j], 16 * (r + 1))
                        if h == 0:
                            dve.wait_ge(query_ready, step + 1)
                        q = query[k][:, h * HT * D:(h + 1) * HT * D].rearrange("p (t d) -> p t d", t=HT)
                        nc.vector.tensor_tensor(key_sb[j][:, :, :, :], key_sb[j][:, :, :, :],
                                                q.unsqueeze(2).to_broadcast([P, HT, LI, D]),
                                                ALU.mult).then_inc(multiplied, 1)
                        dve.wait_ge(multiplied, half + 1)
                        nc.vector.tensor_reduce(out=dots[:, k, h * HT * LI:(h + 1) * HT * LI],
                                                in_=key_sb[j][:, :, :, :].rearrange("p t i d -> p (t i) d"),
                                                axis=AX.X, op=ALU.add).then_inc(summed, 1)
                    if k == 1:
                        invert(r, 0)
                    elif not first:
                        invert(r - 1, 1)
                    dve.wait_ge(summed, HALVES * r + 2 * k + 2)
                    dve.wait_ge(bias_ready, step + 1)
                    if not first:
                        dve.wait_ge(exps_ready, RT * (r - 1) + ST * (k + 1))
                    nc.vector.scalar_tensor_tensor(
                        out=scores[:, k, :, :].rearrange("p t i -> p (t i)"), in0=dots[:, k, :], scalar=SCALE,
                        in1=mask_bias[:, k, :], op0=ALU.mult, op1=ALU.add).then_inc(masked, 1)
                    dve.wait_ge(masked, step + 1)
                    nc.vector.tensor_reduce(out=peak[:, k, 0:ST], in_=scores[:, k, :, :],
                                            axis=AX.X, op=ALU.max).then_inc(peaked, 1)
                    dve.wait_ge(peaked, step + 1)
                    nc.vector.transpose(peak_t[:, k, :], peak[:, k, :]).then_inc(turned, 1)
                    dve.wait_ge(turned, step + 1)
                    nc.vector.tensor_reduce(out=batch_peak[:, k, :],
                                            in_=peak_t[:, k, :].rearrange("p (m o) -> p m o", o=PARTS),
                                            axis=AX.X, op=ALU.max, negate=True).then_inc(grouped, 1)
                    dve.wait_ge(grouped, step + 1)
                    nc.vector.transpose(shift[:, k, :],
                                        batch_peak[:, k, :].unsqueeze(2).to_broadcast([P, SQ // PARTS, PARTS])
                                        ).then_inc(shift_ready, 1)

            def weigh_values(n):
                k, t = divmod(LATE[n], ST)
                dve.wait_ge(late_weights, k + 1)
                dve.wait_ge(values_in[2 * k + t // HT], 16 * ROUNDS)
                v = value_sb[2 * k + t // HT][:, t % HT, :].rearrange("p (i d) -> p i d", d=D)
                w = query[k][:, t * LI:(t + 1) * LI]
                nc.vector.tensor_tensor(v, v, w.unsqueeze(2).to_broadcast([P, LI, D]),
                                        ALU.mult).then_inc(weighted, 1)
                dve.wait_ge(weighted, n + 1)
                nc.vector.tensor_reduce(out=partial[:, n, :], in_=v.rearrange("p i d -> p d i"),
                                        axis=AX.X, op=ALU.add).then_inc(partial_ready, 1)

            rounds(dve, body)
            for n, tile in enumerate(LATE):
                if n == sum(x < ST for x in LATE):
                    invert(ROUNDS - 1, 1)
                weigh_values(n)

        @block.scalar
        def _(act):
            act.wait_ge(folded, 1)
            nc.scalar.copy(w_query[:, :], denom_ps[0:D, 0:D]).then_inc(folded_copied, 1)

            def copy_target(n):
                act.wait_ge(turned_target, n + 1)
                if n == 0:
                    rows = target_t[:, 0:P * HEAD].rearrange("d (p x) -> d x p", x=HEAD)
                else:
                    rows = target_t[:, P * HEAD:].rearrange("d (p x) -> d x p", x=REST)[:, HEAD * (n - 1):HEAD * n, :]
                nc.scalar.copy(rows, cross[n % 2][0:D, :].rearrange("d (x p) -> d x p", x=HEAD)).then_inc(target_copied, 1)

            def spread_target(r, k, cols, first):
                if not first:
                    act.wait_ge(query_ready, 2 * (r - 1) + k + 1)
                nc.scalar.copy(target_rep[:, k, :, :],
                               cols.unsqueeze(2).to_broadcast([D, P // 2, PARTS])).then_inc(target_spread, 1)

            def cast_mask(r, first):
                act.wait_ge(mask_in, 16 * (r + 1))
                if not first:
                    act.wait_ge(mask_placed, r)
                nc.scalar.copy(mask_f[:, :, :], mask_raw[:, :, :]).then_inc(mask_cast, 1)

            def convert_mask(r, k, first):
                if k == 0:
                    act.wait_ge(mask_placed, r + 1)
                if not first:
                    act.wait_ge(masked, 2 * r + k - 1)
                nc.scalar.activation(mask_bias[:, k, :], mask_ps[:, k * ST * LI:(k + 1) * ST * LI],
                                     ACT.Copy, bias=-MASKED, scale=MASKED).then_inc(bias_ready, 1)

            copy_target(0)
            act.wait_ge(target_copied, 1)
            for k in range(2):
                spread_target(0, k, target_t[:, k * P // 2:(k + 1) * P // 2], True)
            cast_mask(0, True)
            convert_mask(0, 0, True)
            convert_mask(0, 1, True)
            cast_mask(1, False)
            for n in range(1, ROUNDS // HEAD):
                copy_target(n)
            for k in range(2):
                spread_target(1, k, target_t[:, P + k * P // 2:P + (k + 1) * P // 2], False)
            act.wait_ge(turned_wv, 1)
            nc.scalar.copy(wv_t[:, :], out_ps[0:D, 0:D]).then_inc(wv_copied, 1)
            act.wait_ge(target_copied, ROUNDS // HEAD)

            def exps(r, k, first):
                act.wait_ge(shift_ready, 2 * r + k + 1)
                if not first:
                    act.wait_ge(spread_ready, HALVES * (r - 1) + 2 * (k + 1))
                    act.wait_ge(denom_ready, 2 * (r - 1) + k + 1)
                for t in range(ST):
                    nc.scalar.activation(weights[:, k, t, :], scores[:, k, t, :], ACT.Exp,
                                         bias=shift[:, k, t:t + 1], scale=1.0,
                                         accum_out=weight_sum[:, k, t:t + 1]).then_inc(exps_ready, 1)

            def keep_weights(k):
                act.wait_ge(multiplied, HALVES * (ROUNDS - 1) + 2 * (k + 1))
                act.wait_ge(exps_ready, RT * (ROUNDS - 1) + ST * (k + 1))
                nc.scalar.copy(query[k][:, 0:ST * LI],
                               weights[:, k, :, :].rearrange("p t i -> p (t i)")).then_inc(late_weights, 1)

            exps(0, 0, True)

            def copy_mixed(r):
                act.wait_ge(picked, RT * (r + 1))
                nc.scalar.copy(mixed[:, :], mixed_ps[0:D, 0:P]).then_inc(mixed_copied, 1)

            def store_out(r):
                act.wait_ge(out_ready, r + 1)
                nc.scalar.copy(out_sb[:, :], out_ps[:, 0:D]).then_inc(out_copied, 1)
                act.wait_ge(out_copied, r + 1)
                act.dma_start(out_v[r], out_sb[:, :]).then_inc(out_stored, 16)

            def body(r, first, left):
                for k in range(2):
                    for t in range(ST):
                        tile = RT * r + ST * k + t
                        act.wait_ge(cross_ready, tile + 1)
                        if t == 0:
                            act.wait_ge(recip_ready, 2 * r + k + 1)
                        if not (first and k == 0 and t < 2):
                            act.wait_ge(picked, tile - 1)
                        m, d = (TB, D) if late(left, k, t) else (JM, JD)
                        nc.scalar.mul(crossed[0:m, t % 2, 0:d], cross[t % 2][0:m, 0:d],
                                      recip[0:m, k, t:t + 1]).then_inc(cross_copied, 1)
                        if k == 0 and t == 0 and not first:
                            copy_mixed(r - 1)
                        if k == 0 and t == 1 and not first:
                            store_out(r - 1)
                        if t == 1:
                            if k == 0:
                                exps(r, 1, first)
                                if not left:
                                    keep_weights(1)
                            elif left:
                                exps(r + 1, 0, False)
                                if left == 1:
                                    keep_weights(0)
                        if t == 1 and left:
                            convert_mask(r + 1, k, False)
                        if t == 2 and k == 1 and left == 2:
                            cast_mask(r + 2, False)
                        if t == 1 and left == 2:
                            b0 = (r + 2) * P + k * P // 2
                            spread_target(r + 2, k, target_t[:, bass.ds(b0, P // 2)], False)

                if not first:
                    act.wait_ge(out_stored, 16 * r)

            rounds(act, body)
            copy_mixed(ROUNDS - 1)
            store_out(ROUNDS - 1)
            act.wait_ge(out_stored, 16 * ROUNDS)

        @block.tensor
        def _(pe):
            def make_query(r, k, first):
                pe.wait_ge(target_spread, 2 * r + k + 1)
                if not first:
                    pe.wait_ge(multiplied, HALVES * (r - 1) + 2 * (k + 1))
                for t in range(ST):
                    last = nc.tensor.matmul(query[k][:, t * D:(t + 1) * D],
                                            target_rep[:, k, t * TB:(t + 1) * TB, :].rearrange("d b o -> d (b o)"),
                                            w_query[:, :], start=True, stop=True)
                last.then_inc(query_ready, 1)

            def turn_target(n):
                if n >= 2:
                    pe.wait_ge(target_copied, n - 1)
                for x in range(HEAD):
                    last = nc.tensor.transpose(cross[n % 2][0:D, x * P:(x + 1) * P],
                                               target_sb[:, HEAD * n + x, :], ident[:, :])
                last.then_inc(turned_target, 1)

            def place_mask(r, first):
                if not first:
                    pe.wait_ge(bias_ready, 2 * r)
                pe.wait_ge(mask_cast, r + 1)
                for x in range(RUN_PARTS):
                    last = nc.tensor.matmul(mask_ps[:, 0:RT * LI], place[:, x, :],
                                            mask_f[:, :, x * LI:(x + 1) * LI], start=(x == 0), stop=(x == RUN_PARTS - 1))
                last.then_inc(mask_placed, 1)

            pe.wait_ge(ident_ready, 1)
            pe.wait_ge(weights_in, 32)
            nc.tensor.matmul(denom_ps[0:D, 0:D], wt_sb[:, :], wi_sb[:, :], start=True, stop=True).then_inc(folded, 1)
            pe.wait_ge(target_in, 16)
            turn_target(0)
            pe.wait_ge(folded_copied, 1)
            make_query(0, 0, True)
            make_query(0, 1, True)
            pe.wait_ge(place_ready, 1)
            place_mask(0, True)
            pe.wait_ge(wv_in, 16)
            nc.tensor.transpose(out_ps[0:D, 0:D], wv_sb[:, :], ident[0:D, 0:D]).then_inc(turned_wv, 1)
            pe.wait_ge(target_rest_in, 16)
            for n in range(1, ROUNDS // HEAD):
                turn_target(n)
            pe.wait_ge(target_copied, ROUNDS // HEAD)
            pe.wait_ge(wv_copied, 1)
            pe.wait_ge(own_rep_ready, 1)

            def cross_products(r, k, t, first):
                tile = RT * r + ST * k + t
                j, h = 2 * k + t // HT, t // HT
                if t % HT == 0:
                    pe.wait_ge(spread_ready, HALVES * r + j + 1)
                    pe.wait_ge(values_in[j], 16 * (r + 1))
                if not (first and k == 0 and t < 2):
                    pe.wait_ge(cross_copied, tile - 1)
                for g in range(GROUPS):
                    last = nc.tensor.matmul(
                        cross[t % 2][0:JM, 0:JD],
                        spread[:, k, t, g * J:(g + 1) * J, :].rearrange("p i m -> p (i m)"),
                        value_sb[j][:, t % HT, g * JD:(g + 1) * JD], start=(g == 0), stop=(g == GROUPS - 1))
                last.then_inc(cross_ready, 1)

            def sum_parts(k, t):
                tile, n = RT * (ROUNDS - 1) + ST * k + t, LATE.index(ST * k + t)
                pe.wait_ge(partial_ready, n + 1)
                pe.wait_ge(cross_copied, tile - 1)
                nc.tensor.matmul(cross[t % 2][0:TB, 0:D], own[:, :], partial[:, n, :],
                                 start=True, stop=True).then_inc(cross_ready, 1)

            def pick(r, k, t, first, blocks=J):
                tile = RT * r + ST * k + t
                pe.wait_ge(cross_copied, tile + 1)
                if k == 0 and t == 0 and not first:
                    pe.wait_ge(mixed_copied, r)
                b0 = (ST * k + t) * TB
                for x in range(blocks):
                    last = nc.tensor.matmul(mixed_ps[0:D, b0:b0 + TB], crossed[0:blocks * TB, t % 2, x * D:(x + 1) * D],
                                            ident[0:blocks * TB, x * TB:(x + 1) * TB],
                                            start=(x == 0), stop=(x == blocks - 1))
                last.then_inc(picked, 1)

            def denominators(r, k, first):
                pe.wait_ge(exps_ready, RT * r + ST * (k + 1))
                if not (first and k == 0):
                    pe.wait_ge(recip_ready, 2 * r + k)
                nc.tensor.matmul(denom_ps[0:JM, ST * k:ST * (k + 1)],
                                 own_rep[:, :, :].rearrange("p j m -> p (j m)"),
                                 weight_sum[:, k, :], start=True, stop=True).then_inc(denom_ready, 1)

            def project(r):
                pe.wait_ge(mixed_copied, r + 1)
                nc.tensor.matmul(out_ps[:, 0:D], mixed[:, :], wv_t[:, :], start=True, stop=True).then_inc(out_ready, 1)

            make_query(1, 0, False)
            denominators(0, 0, True)

            def body(r, first, left):
                for k in range(2):
                    if k == 0 and left:
                        make_query(r + 1, 1, False)
                    elif k == 1 and left == 2:
                        make_query(r + 2, 0, False)
                    for t in range(ST):
                        if late(left, k, t):
                            sum_parts(k, t)
                        else:
                            cross_products(r, k, t, first)
                        if t == 0 and k == 0 and left:
                            place_mask(r + 1, False)
                        if t == ST - 1:
                            if k == 0:
                                denominators(r, 1, first)
                            elif left:
                                denominators(r + 1, 0, False)
                        if t == 1 and k == 0 and not first:
                            project(r - 1)
                        if t > 0:
                            pick(r, k, t - 1, first, 1 if late(left, k, t - 1) else J)
                        elif k == 1:
                            pick(r, 0, ST - 1, first, 1 if late(left, 0, ST - 1) else J)
                        elif not first:
                            pick(r - 1, 1, ST - 1, False)

            rounds(pe, body)
            pick(ROUNDS - 1, 1, ST - 1, False, 1)
            project(ROUNDS - 1)


_INS = ["r_target_key", "r_item_keys", "r_item_values", "r_mask",
        "L0_rec_W_target", "L0_rec_W_item", "L0_rec_W_value"]


def kernel(**inputs):
    import numpy as np
    import concourse.bacc as bacc
    from concourse.bass_utils import run_bass_kernel_spmd

    nc = bacc.Bacc("TRN2", target_bir_lowering=False, num_devices=1)
    arrays, args = {}, []
    for name in _INS:
        a = np.ascontiguousarray(inputs[name])
        arrays[f"in_{name}"] = a
        args.append(nc.dram_tensor(f"in_{name}", a.shape, mybir.dt.from_np(a.dtype), kind="ExternalInput").ap())
    out = nc.dram_tensor("out", inputs["r_target_key"].shape, mybir.dt.float32, kind="ExternalOutput").ap()
    target_attention(nc, *args, out)
    r = run_bass_kernel_spmd(nc, [arrays], core_ids=[0])
    return r.results[0]["out"]
```
